# Optimizing a Trainium2 kernel written in Bass

```python
import numpy as np
import jax
import jax.numpy as jnp

def _softmax(x, axis=-1):
    return jax.nn.softmax(x, axis=axis)

def _gelu(x):
    return jax.nn.gelu(x, approximate=True)

def _silu(x):
    return jax.nn.silu(x)

def _sigmoid(x):
    return jax.nn.sigmoid(x)

def _layernorm(x, axis=-1, eps=1e-05):
    m = jnp.mean(x, axis=axis, keepdims=True)
    v = jnp.var(x, axis=axis, keepdims=True)
    return (x - m) / jnp.sqrt(v + eps)

def _scatter_add(tgt, idx, src, axis=0):
    return tgt.at[idx].add(src)

def _segment_sum(src, seg, n):
    return jax.ops.segment_sum(src, seg, n)
kernel_name = 'mk_gnn_ffn_d1_gnn_r32_e8da1f'

def setup_inputs(seed: int=0):
    np.random.seed(seed)
    _w = jnp.asarray

    def _rec_inputs():
        import jax
        import jax.numpy as jnp
        _gk = jax.random.key(seed)
        x = -0.0002117 + 1 * jax.random.normal(jax.random.fold_in(_gk, 1), (3125, 256), jnp.float32)
        _s = jax.random.randint(jax.random.fold_in(_gk, 2), (25000,), 0, 3125, jnp.int32)
        _d = jax.random.randint(jax.random.fold_in(_gk, 3), (25000,), 0, 3125, jnp.int32)
        _loop = jnp.arange(3125, dtype=jnp.int32)
        src = jnp.concatenate([_s, _d, _loop])
        dst = jnp.concatenate([_d, _s, _loop])
        _o = jnp.argsort(dst, stable=True)
        src = src[_o]
        dst = dst[_o]
        return (x, src, dst)
    x, src, dst = _rec_inputs()

    def _L0_gnn_setup():
        import jax, jax.numpy as jnp
        import numpy as np
        N = 3125
        E = 50000
        D = 256
        BN_EPS = 1e-05
        key = jax.random.key(seed)
        ks = jax.random.split(key, 6)
        node_feats = jax.random.normal(ks[0], (N, D), dtype=jnp.float32)
        src = jax.random.randint(ks[1], (E,), 0, N, dtype=jnp.int64)
        dst = jax.random.randint(ks[2], (E,), 0, N, dtype=jnp.int64)
        eps = jnp.zeros((1,), dtype=jnp.float32)
        W1 = jax.random.normal(ks[3], (D, 2 * D), dtype=jnp.float32) * (1.0 / np.sqrt(D))
        b1 = jnp.zeros((2 * D,), dtype=jnp.float32)
        W2 = jax.random.normal(ks[4], (2 * D, D), dtype=jnp.float32) * (1.0 / np.sqrt(2 * D))
        b2 = jnp.zeros((D,), dtype=jnp.float32)
        gamma = jnp.ones((D,), dtype=jnp.float32)
        beta = jnp.zeros((D,), dtype=jnp.float32)
        return {'node_feats': node_feats, 'src': src, 'dst': dst, 'eps': eps, 'W1': W1, 'b1': b1, 'W2': W2, 'b2': b2, 'gamma': gamma, 'beta': beta}
    _L0_gnn_all = _L0_gnn_setup()
    _L0_gnn_in = {k: v for k, v in _L0_gnn_all.items() if k in ('eps', 'W1', 'b1', 'W2', 'b2', 'gamma', 'beta')}
    del _L0_gnn_all

    def _L0_ffn_setup():
        import jax, jax.numpy as jnp
        import numpy as np
        TOP_K = 2
        key = jax.random.key(seed)
        ks = jax.random.split(key, 4)
        B, L, D, H, E = (8, 128, 256, 1024, 8)
        s = 0.02
        return {'x': jax.random.normal(ks[0], (B, L, D), jnp.float32), 'Wg': jax.random.normal(ks[1], (D, E), jnp.float32) * s, 'bg': jnp.zeros((E,), jnp.float32), 'W1': jax.random.normal(ks[2], (E, D, H), jnp.float32) * s, 'b1': jnp.zeros((E, H), jnp.float32), 'W2': jax.random.normal(ks[3], (E, H, D), jnp.float32) * s, 'b2': jnp.zeros((E, D), jnp.float32)}
    _L0_ffn_all = _L0_ffn_setup()
    _L0_ffn_in = {k: v for k, v in _L0_ffn_all.items() if k in ('Wg', 'bg', 'W1', 'b1', 'W2', 'b2')}
    del _L0_ffn_all
    return {'x': x, 'src': src, 'dst': dst, 'L0_gnn_eps': _L0_gnn_in['eps'], 'L0_gnn_W1': _L0_gnn_in['W1'], 'L0_gnn_b1': _L0_gnn_in['b1'], 'L0_gnn_W2': _L0_gnn_in['W2'], 'L0_gnn_b2': _L0_gnn_in['b2'], 'L0_gnn_gamma': _L0_gnn_in['gamma'], 'L0_gnn_beta': _L0_gnn_in['beta'], 'L0_ffn_Wg': _L0_ffn_in['Wg'], 'L0_ffn_bg': _L0_ffn_in['bg'], 'L0_ffn_W1': _L0_ffn_in['W1'], 'L0_ffn_b1': _L0_ffn_in['b1'], 'L0_ffn_W2': _L0_ffn_in['W2'], 'L0_ffn_b2': _L0_ffn_in['b2']}

def reference(x, src, dst, L0_gnn_eps, L0_gnn_W1, L0_gnn_b1, L0_gnn_W2, L0_gnn_b2, L0_gnn_gamma, L0_gnn_beta, L0_ffn_Wg, L0_ffn_bg, L0_ffn_W1, L0_ffn_b1, L0_ffn_W2, L0_ffn_b2):
    import jax
    import jax.numpy as jnp

    def _L0_gnn_ref(node_feats, src, dst, eps, W1, b1, W2, b2, gamma, beta):
        import jax, jax.numpy as jnp
        import numpy as np
        N = 3125
        E = 50000
        D = 256
        BN_EPS = 1e-05
        n = node_feats.shape[0]
        neigh = jax.ops.segment_sum(node_feats[src], dst, num_segments=n)
        h = (1.0 + eps) * node_feats + neigh
        h = jax.nn.relu(h @ W1 + b1) @ W2 + b2
        mean = jnp.mean(h, axis=0)
        var = jnp.mean(jnp.square(h - mean), axis=0)
        h = (h - mean) * jax.lax.rsqrt(var + BN_EPS) * gamma + beta
        return h

    def _L0_ffn_ref(x, Wg, bg, W1, b1, W2, b2):
        import jax, jax.numpy as jnp
        import numpy as np
        TOP_K = 2
        B, L, D = x.shape
        E = W1.shape[0]
        xf = x.reshape(-1, D)
        gate_logits = xf @ Wg + bg
        top_w, top_i = jax.lax.top_k(gate_logits, TOP_K)
        top_w = jax.nn.softmax(top_w, axis=-1)
        w_dense = jnp.sum(jax.nn.one_hot(top_i, E, dtype=xf.dtype) * top_w[..., None], axis=1)
        out = jnp.zeros_like(xf)
        for e in range(E):
            h = jax.nn.gelu(xf @ W1[e] + b1[e], approximate=False)
            out = out + w_dense[:, e:e + 1] * (h @ W2[e] + b2[e])
        return out.reshape(B, L, D)
    x = x + _L0_gnn_ref(_layernorm(x, axis=-1), src, dst, L0_gnn_eps, L0_gnn_W1, L0_gnn_b1, L0_gnn_W2, L0_gnn_b2, L0_gnn_gamma, L0_gnn_beta)
    x = x + _L0_ffn_ref(_layernorm(x, axis=-1)[None], L0_ffn_Wg, L0_ffn_bg, L0_ffn_W1, L0_ffn_b1, L0_ffn_W2, L0_ffn_b2)[0]
    return x

_drawn_inputs = setup_inputs


def setup_inputs(seed=0):
    import zlib

    import numpy as np

    out = dict(_drawn_inputs(seed))
    spreads = {'L0_gnn_b1': (0.0, 0.481),
     'L0_gnn_b2': (0.0, 0.8),
     'L0_gnn_gamma': (1.0, 0.2),
     'L0_gnn_beta': (0.0, 0.1),
     'L0_ffn_bg': (0.0, 0.1),
     'L0_ffn_b1': (0.0, 0.43),
     'L0_ffn_b2': (0.0, 0.1)}
    factors = {}
    for name, (base, spread) in spreads.items():
        noise = np.random.default_rng([zlib.crc32(name.encode()), seed]).standard_normal(out[name].shape)
        drawn = base * np.exp(spread * noise) if base else spread * noise
        out[name] = jnp.asarray(drawn.astype(out[name].dtype))
    for name, factor in factors.items():
        out[name] = (out[name] * factor).astype(out[name].dtype)
    return out
```

```python
import concourse.bass as bass
from concourse import mybir
from contextlib import ExitStack


def gnn_moe_block(nc, x, src, dst, eps, g_w1, g_b1, g_w2, g_b2, gamma, beta,
                  wg, bg, e_w1, e_b1, e_w2, e_b2, out):
    fp32 = mybir.dt.float32
    i32 = mybir.dt.int32
    ALU = mybir.AluOpType
    ACT = mybir.ActivationFunctionType
    AX = mybir.AxisListType

    N, D = x.shape
    E = src.shape[0]
    NE, _, H = e_w1.shape
    GH = g_w1.shape[1]
    P = 128
    K = D // P
    GM = GH // P
    EM = H // P
    T = -(-N // P)
    NP = T * P
    LAST = N - (T - 1) * P
    CH = 4
    GE = CH * P
    G = -(-E // GE)
    GFULL = E // GE
    GREST = E - GFULL * GE
    W = 64
    SLOTS = 4
    assert G % SLOTS == 0 and G <= P and GREST > 0
    FAR = 8192.0
    PIECE = 5
    NPIECE = T // PIECE
    MG = 8
    MC = NP // MG
    MLAST = N - (MG - 1) * MC
    RT = 256
    RH = RT // P
    CAP = (-(-N // RT) + 1) * RT
    ROW = D + 4
    META = D
    BIG = 1.0e6
    BN_EPS = 1e-5
    WOPS = 7

    xn_dram = nc.dram_tensor("xn_dram", [NP, D], fp32, kind="Internal").ap()
    slots_dram = nc.dram_tensor("slots_dram", [NE * CAP, ROW], fp32, kind="Internal").ap()
    y_dram = nc.dram_tensor("y_dram", [2 * NP, D], fp32, kind="Internal").ap()

    ctx = ExitStack()
    with ctx:
        def sb(name, shape, dt=fp32):
            return ctx.enter_context(nc.sbuf_tensor(name, shape, dt))

        def sem(name):
            return ctx.enter_context(nc.semaphore(name))

        x_sb = sb("x_sb", [P, T, D])
        xn = sb("xn", [P, T, ROW])
        agg = sb("agg", [P, K, NP + W])
        ident = sb("ident", [P, P])
        ones = sb("ones", [P, P])
        upper = sb("upper", [P, P])
        iota_n = sb("iota_n", [P, NP])
        rows_all = sb("rows_all", [P, SLOTS, CH * D])
        rows = [rows_all[:, s, :].rearrange("p (c d) -> p c d", d=D) for s in range(SLOTS)]
        near = [sb(f"near{s}", [P, CH, W]) for s in range(SLOTS)]
        onehot = [sb(f"onehot{s}", [P, CH, W]) for s in range(SLOTS)]
        idx = [sb(f"idx{s}", [P, CH], i32) for s in range(SLOTS)]
        src_i = sb("src_i", [G, GE], i32)
        dst_i = sb("dst_i", [G, GE], i32)
        src_f = sb("src_f", [G, GE])
        dst_f = sb("dst_f", [G, GE])
        dst_real = sb("dst_real", [G, GE])
        dminmax = sb("dminmax", [G, 2])
        dspread = sb("dspread", [G, 2, P])
        wmin = sb("wmin", [P, G])
        span = sb("span", [P, G])
        rem = sb("rem", [P, G])
        steps = sb("steps", [P, G])
        srcT = sb("srcT", [P, G * CH])
        below = sb("below", [P, G * CH])
        tab_step = sb("tab_step", [P, G + 1], i32)
        tab_win = sb("tab_win", [P, G], i32)
        stats = sb("stats", [P, T, 6])
        mv = sb("mv", [P, T, 2])
        rstd = sb("rstd", [P, T])
        nbias = sb("nbias", [P, T])
        veps = sb("veps", [P, T])
        nmean = sb("nmean", [P, T])
        halves = sb("halves", [P, T])
        gw1 = sb("gw1", [P, K, GH])
        gw2 = sb("gw2", [P, GM, D])
        hid = iota_n[:, 0:GM * MC].rearrange("p (m c) -> p m c", c=MC)
        bnst = sb("bnst", [P, K, MG, 6])
        bnmv = sb("bnmv", [P, K, 2])
        bnsc = sb("bnsc", [P, K])
        bnsh = sb("bnsh", [P, K])
        NB = NE * EM + GM + 3 * K
        brows = sb("brows", [NB, P])
        bcol = sb("bcol", [P, NB])
        B_G1, B_G2, B_GA, B_BE = NE * EM, NE * EM + GM, NE * EM + GM + K, NE * EM + GM + 2 * K
        epsb = sb("epsb", [P, 1])
        bgb = sb("bgb", [P, NE])
        b2b = sb("b2b", [P, NE, D])
        wgs = sb("wgs", [P, K, NE])
        xT = [sb(f"xT{b}", [P, K, P]) for b in range(2)]
        lg = sb("lg", [P, T, NE])
        lg2 = sb("lg2", [P, T, NE])
        eqs = sb("eqs", [P, T, NE])
        m1 = sb("m1", [P, T, NE])
        m2 = sb("m2", [P, T, NE])
        msum = sb("msum", [P, T, NE])
        tot = sb("tot", [P, T, NE])
        incl = sb("incl", [P, T, NE])
        posn = sb("posn", [P, T, NE])
        v1 = sb("v1", [P, T])
        v2 = sb("v2", [P, T])
        r1 = sb("r1", [P, T])
        r2 = sb("r2", [P, T])
        ex = sb("ex", [P, T])
        w1v = sb("w1v", [P, T])
        w2v = sb("w2v", [P, T])
        valid = sb("valid", [P, T])
        novalid = sb("novalid", [P, T])
        posf = sb("posf", [P, 2, T])
        posi = sb("posi", [P, 2, T], i32)
        rank_e = sb("rank_e", [P, NE])
        eoff = sb("eoff", [P, NE])
        tok = sb("tok", [P, T])
        cnt = sb("cnt", [P, NE])
        ntl = sb("ntl", [P, NE])
        padf = sb("padf", [P, NE])
        tab_tile = sb("tab_tile", [P, NE + 1], i32)
        tab_pad = sb("tab_pad", [P, NE], i32)
        padrow = sb("padrow", [P, RH, ROW])
        w1s = [sb(f"w1s{b}", [P, K, H]) for b in range(2)]
        w2s = [sb(f"w2s{b}", [P, EM, D]) for b in range(2)]
        xs = sb("xs", [P, RH, ROW])
        hT = rows_all[:, 0:2, :].rearrange("p s (m c) -> p (s m) c", c=RT)
        xsT = rows_all[:, 2, 0:K * RT].rearrange("p (k c) -> p k c", c=RT)
        ytmp = rows_all[:, 2, K * RT:K * RT + RH * D].rearrange("p (a d) -> p a d", d=D)
        ysb = rows_all[:, 3, 0:RH * D].rearrange("p (a d) -> p a d", d=D)
        meta = sb("meta", [P, 2, RH * 4])
        is1 = sb("is1", [P, RH])
        not1 = sb("not1", [P, RH])
        wa = sb("wa", [P, RH])
        wsel = sb("wsel", [P, RH])
        dest = sb("dest", [P, RH])
        desti = sb("desti", [P, RH], i32)

        ps = [ctx.enter_context(nc.psum_tensor(f"ps{b}", [P, 512], fp32)) for b in range(8)]

        l_edges, l_small, l_gw, l_pads = sem("l_edges"), sem("l_small"), sem("l_gw"), sem("l_pads")
        l_x = [sem(f"l_x{q}") for q in range(NPIECE)]
        l_w = [sem(f"l_w{b}") for b in range(2)]
        xn_stored = sem("xn_stored")
        pads_set, x_pad_set, consts, pool_seq, dve_seq, act_seq = (
            sem(n) for n in ("pads_set", "x_pad_set", "consts", "pool_seq", "dve_seq", "act_seq"))
        dst_ready, src_ready, lists_T, table_ready, bias_T, bias_ready = (
            sem(n) for n in ("dst_ready", "src_ready", "lists_T", "table_ready", "bias_T", "bias_ready"))
        mv_ready, rstd_ready, xn_ready, xn_T, agg_set = (
            sem(n) for n in ("mv_ready", "rstd_ready", "xn_ready", "xn_T", "agg_set"))
        slot_free, idx_ready, near_ready, onehot_ready, win_mm, win_done = (
            sem(n) for n in ("slot_free", "idx_ready", "near_ready", "onehot_ready", "win_mm", "win_done"))
        rows_in = [sem(f"rows_in{s}") for s in range(SLOTS)]
        mm1_done, relu_done, mm2_done, h_done, bn_ready, bn_var, bn_rstd = (
            sem(n) for n in ("mm1_done", "relu_done", "mm2_done", "h_done", "bn_ready", "bn_var", "bn_rstd"))
        bn_applied, h_T, res_done, mv2_ready, rstd2_ready, xn2_ready, xn2_T, xT_ready, gate_done = (
            sem(n) for n in ("bn_applied", "h_T", "res_done", "mv2_ready", "rstd2_ready", "xn2_ready", "xn2_T",
                             "xT_ready", "gate_done"))
        diff_ready, exp_ready, mask_ready, rank_mm, route_ready, slots_in, pads_in = (
            sem(n) for n in ("diff_ready", "exp_ready", "mask_ready", "rank_mm", "route_ready", "slots_in", "pads_in"))
        xs_in, xs_T, xsT_ready, meta_ready, e_mm1, gelu_done, e_mm2, expert_done, wsel_ready, y_ready, ybuf_free = (
            sem(n) for n in ("xs_in", "xs_T", "xsT_ready", "meta_ready", "e_mm1", "gelu_done", "e_mm2",
                             "expert_done", "wsel_ready", "y_ready", "ybuf_free"))
        pool_waited = sem("pool_waited")
        y_out, y_seq, bn_chunks = sem("y_out"), sem("y_seq"), sem("bn_chunks")
        y_in = [sem(f"y_in{q}") for q in range(NPIECE)]
        out_ready, out_stored = sem("out_ready"), sem("out_stored")

        block = ctx.enter_context(nc.Block())

        def rows_of(t0, t1):
            return slice(t0 * P, t1 * P)

        def piece_io(eng, sems, load, t0, t1, dram, tile):
            full = min(t1, T - 1)
            a, b = tile[:, t0:full, 0:D], dram[rows_of(t0, full), :].rearrange("(t p) d -> p t d", p=P)
            eng.dma_start(*((a, b) if load else (b, a))).then_inc(sems, 16)
            if t1 == T:
                a, b = tile[0:LAST, T - 1, 0:D], dram[(T - 1) * P:N, :]
                eng.dma_start(*((a, b) if load else (b, a))).then_inc(sems, 16)

        def table(eng, tab, i, lo, hi):
            return eng.value_load(tab[0:1, bass.ds(i, 1)], min_val=lo, max_val=hi)

        MAXSTEP = G * (NP // W + 1) + 1
        MAXTILE = NE * (-(-N // RT)) + 1

        def window(first, step, first_step, most):
            return nc.s_assert_within(first + (step - first_step) * W, 0, most,
                                      skip_runtime_bounds_check_because="a window starts at or before the last node")

        def extra_steps(eng, s0, s1, body):
            with eng.If(s1 > s0 + 1):
                with eng.Fori(s0 + 1, s1) as s:
                    body(s)
            eng.nop()

        def y_pair(t0, t1):
            second = agg[:, :, :].rearrange("p k n -> p (k n)")[:, 0:T * D].rearrange("p (t d) -> p t d", d=D)
            return xn[:, t0:t1, 0:D], second[:, t0:t1, :]

        def copy_xT(act, t):
            act.wait_ge(xn2_T, t + 1)
            if t >= 2:
                act.wait_ge(gate_done, t - 1)
            act.activation(xT[t % 2][:, :, :], ps[4 + t % 2][:, 0:K * P].rearrange("p (k c) -> p k c", c=P), ACT.Copy)\
               .then_inc(xT_ready, 1)

        @block.sync
        def _(sp):
            sp.wait_ge(pads_set, 2)
            for i, (lst, dram) in enumerate(((dst_i, dst), (src_i, src))):
                sp.dma_start(lst[0:GFULL, :], dram[0:GFULL * GE].rearrange("(g e) -> g e", e=GE)).then_inc(l_edges, 16)
                sp.dma_start(lst[GFULL:G, 0:GREST], dram[GFULL * GE:E].rearrange("(g e) -> g e", g=1)).then_inc(l_edges, 16)
            for q in range(NPIECE):
                if q == NPIECE - 1:
                    sp.wait_ge(x_pad_set, 1)
                piece_io(sp, l_x[q], True, q * PIECE, (q + 1) * PIECE, x, x_sb)
            sp.dma_start(brows[0:B_G1, :], e_b1.rearrange("e (m p) -> (e m) p", p=P)).then_inc(l_small, 16)
            for at, v in ((B_G1, g_b1), (B_G2, g_b2), (B_GA, gamma), (B_BE, beta)):
                n = v.shape[0] // P
                sp.dma_start(brows[at:at + n, :], v.rearrange("(m p) -> m p", p=P)).then_inc(l_small, 16)
            sp.dma_start(bgb[:, :], bg.rearrange("(a e) -> a e", a=1).broadcast_to((P, NE))).then_inc(l_small, 16)
            sp.dma_start(wgs[:, :, :], wg.rearrange("(k p) e -> p k e", p=P)).then_inc(l_small, 16)
            sp.dma_start(gw1[:, :, :], g_w1.rearrange("(k p) h -> p k h", p=P)).then_inc(l_gw, 16)
            sp.dma_start(gw2[:, :, :], g_w2.rearrange("(m p) d -> p m d", p=P)).then_inc(l_gw, 16)
            for q in range(NPIECE):
                sp.wait_ge(xn_ready, (q + 1) * PIECE)
                sp.dma_start(xn_dram[rows_of(q * PIECE, (q + 1) * PIECE), :].rearrange("(t p) d -> p t d", p=P),
                             xn[:, q * PIECE:(q + 1) * PIECE, 0:D]).then_inc(xn_stored, 16)
            sp.dma_start(b2b[:, :, :].rearrange("p e d -> p (e d)"),
                         e_b2.rearrange("(a e) d -> a (e d)", a=1).broadcast_to((P, NE * D))).then_inc(l_gw, 16)

            sp.wait_ge(route_ready, 1)
            for e in range(NE):
                r = table(sp, tab_pad, e, 0, NE * CAP - RT)
                sp.dma_start(slots_dram[bass.ds(r, RT), :].rearrange("(a p) d -> p a d", p=P),
                             padrow[:, :, :]).then_inc(pads_in, 16)

            sp.wait_ge(slots_in, 16 * 2 * T)
            sp.wait_ge(pads_in, 16 * NE)
            for e in range(NE):
                j0 = table(sp, tab_tile, e, 1, MAXTILE)
                j1 = table(sp, tab_tile, e + 1, 1, MAXTILE)
                with sp.Fori(j0, j1) as j:
                    r = nc.s_assert_within((j - j0) * RT + e * CAP, 0, NE * CAP - RT,
                                           skip_runtime_bounds_check_because="a list has at most CAP rows")
                    sp.wait_ge(xs_T, j)
                    sp.wait_ge(meta_ready, j)
                    sp.dma_start(xs[:, :, :], slots_dram[bass.ds(r, RT), :].rearrange("(a p) d -> p a d", p=P))\
                      .then_inc(xs_in, 16)
            jn = table(sp, tab_tile, NE, 1, MAXTILE)
            sp.wait_ge(xs_T, jn)
            sp.wait_ge(meta_ready, jn)
            sp.dma_start(xs[:, :, :], slots_dram[0:RT, :].rearrange("(a p) d -> p a d", p=P)).then_inc(xs_in, 16)

            sp.wait_ge(ybuf_free, jn)
            for q in range(NPIECE):
                t0, t1 = q * PIECE, (q + 1) * PIECE
                ya, yb = y_pair(t0, t1)
                for k, y in ((0, ya), (1, yb)):
                    full = min(t1, T - 1)
                    sp.dma_start(y[:, 0:full - t0, :],
                                 y_dram[k * NP + t0 * P:k * NP + full * P, :].rearrange("(t p) d -> p t d", p=P))\
                      .then_inc(y_in[q], 16)
                    if t1 == T:
                        sp.dma_start(y[0:LAST, T - 1 - t0, :], y_dram[k * NP + (T - 1) * P:k * NP + N, :])\
                          .then_inc(y_in[q], 16)
            for q in range(NPIECE):
                sp.wait_ge(out_ready, q + 1)
                piece_io(sp, out_stored, False, q * PIECE, (q + 1) * PIECE, out, x_sb)
            sp.wait_ge(out_stored, 16 * (NPIECE + 1))

        @block.gpsimd
        def _(pool):
            pool.memset(dst_i[:, :], int(FAR)).then_inc(pads_set, 1)
            pool.memset(src_i[:, :], 0).then_inc(pads_set, 1)
            pool.memset(ident[:, :], 0.0).then_inc(pool_seq, 1)
            pool.memset(upper[:, :], 1.0).then_inc(pool_seq, 1)
            pool.memset(valid[:, :], 1.0).then_inc(pool_seq, 1)
            pool.memset(ones[:, :], 1.0).then_inc(consts, 1)
            pool.memset(halves[:, :], -0.5).then_inc(pool_seq, 1)
            pool.wait_ge(pool_seq, 4)
            pool.affine_select(out=ident[:, :], in_=ident[:, :], compare_op=ALU.not_equal, fill=1.0,
                               base=0, pattern=[[-1, P]], channel_multiplier=1).then_inc(consts, 1)
            pool.affine_select(out=upper[:, :], in_=upper[:, :], compare_op=ALU.is_ge, fill=0.0,
                               base=-1, pattern=[[1, P]], channel_multiplier=-1).then_inc(consts, 1)
            pool.affine_select(out=valid[:, :], in_=valid[:, :], compare_op=ALU.is_ge, fill=0.0,
                               base=N - 1, pattern=[[-P, T]], channel_multiplier=-1).then_inc(consts, 1)
            pool.iota(iota_n[:, :], pattern=[[1, NP]], base=0, channel_multiplier=0,
                      allow_small_or_imprecise_dtypes=True).then_inc(consts, 1)
            pool.iota(rank_e[:, :], pattern=[[-1, NE]], base=NE, channel_multiplier=0,
                      allow_small_or_imprecise_dtypes=True).then_inc(consts, 1)
            pool.iota(eoff[:, :], pattern=[[CAP, NE]], base=0, channel_multiplier=0,
                      allow_small_or_imprecise_dtypes=True).then_inc(consts, 1)
            pool.iota(tok[:, :], pattern=[[P, T]], base=0, channel_multiplier=1,
                      allow_small_or_imprecise_dtypes=True).then_inc(consts, 1)
            pool.memset(padrow[:, :, :], 0.0).then_inc(consts, 1)
            pool.wait_ge(consts, 9)
            pool.memset(padrow[:, :, META + 3:META + 4], BIG).then_inc(consts, 1)

            def row_scales(t0, t1, ready, count, done):
                pool.wait_ge(ready, count)
                pool.tensor_scalar(veps[:, t0:t1], mv[:, t0:t1, 1], BN_EPS, None, ALU.add).then_inc(pool_seq, 1)
                pool.tensor_scalar(nmean[:, t0:t1], mv[:, t0:t1, 0], -1.0, None, ALU.mult).then_inc(pool_seq, 1)
                pool.wait_ge(pool_seq, seq[0] + 2)
                pool.tensor_tensor(rstd[:, t0:t1], veps[:, t0:t1], halves[:, t0:t1], ALU.pow).then_inc(pool_seq, 1)
                seq[0] += 3
                pool.wait_ge(pool_seq, seq[0])
                pool.tensor_tensor(nbias[:, t0:t1], nmean[:, t0:t1], rstd[:, t0:t1], ALU.mult).then_inc(done, 1)

            seq = [4]
            for q in range(NPIECE):
                row_scales(q * PIECE, (q + 1) * PIECE, mv_ready, (q + 1) * PIECE, rstd_ready)

            pool.wait_ge(xn_stored, 16 * NPIECE)
            with pool.Fori(0, G // SLOTS) as i:
                for s in range(SLOTS):
                    pool.wait_ge(idx_ready, i * SLOTS + s + 1)
                    pool.sem_inc(pool_waited, 1)
                    for c in range(CH):
                        pool.indirect_dma_start(out=rows[s][:, c, :], out_offset=None, in_=xn_dram[:, :],
                                                in_offset=bass.IndirectOffsetOnAxis(ap=idx[s][:, c:c + 1], axis=0))\
                            .then_inc(rows_in[s], 16)

            pool.wait_ge(bn_var, K)
            pool.tensor_scalar(bnsh[:, :], bnmv[:, :, 1], BN_EPS, None, ALU.add).then_inc(pool_seq, 1)
            seq[0] += 1
            pool.wait_ge(pool_seq, seq[0])
            pool.tensor_tensor(bnsc[:, :], bnsh[:, :], halves[:, 0:K], ALU.pow).then_inc(bn_rstd, 1)
            for q in range(NPIECE):
                row_scales(q * PIECE, (q + 1) * PIECE, mv2_ready, (q + 1) * PIECE, rstd2_ready)

            pool.wait_ge(route_ready, 1)
            for t in range(T):
                for k in range(2):
                    pool.indirect_dma_start(out=slots_dram[:, :], in_=xn[:, t, :], in_offset=None,
                                            out_offset=bass.IndirectOffsetOnAxis(ap=posi[:, k, t:t + 1], axis=0),
                                            bounds_check=NE * CAP - 1, oob_is_err=False).then_inc(slots_in, 16)

            pool.sem_inc(ybuf_free, 1)
            for e in range(NE):
                j0 = table(pool, tab_tile, e, 1, MAXTILE)
                j1 = table(pool, tab_tile, e + 1, 1, MAXTILE)
                with pool.Fori(j0, j1) as j:
                    pool.wait_ge(y_ready, j)
                    pool.sem_inc(pool_waited, 1)
                    for a in range(RH):
                        pool.indirect_dma_start(out=y_dram[:, :], in_=ysb[:, a, :], in_offset=None,
                                                out_offset=bass.IndirectOffsetOnAxis(ap=desti[:, a:a + 1], axis=0),
                                                bounds_check=2 * NP - 1, oob_is_err=False).then_inc(y_out, 16)
                    pool.wait_ge(y_out, j * (16 * RH))
                    pool.sem_inc(ybuf_free, 1)

        @block.scalar
        def _(act):
            for b in range(2):
                act.dma_start(w1s[b][:, :, :], e_w1[b].rearrange("(k p) h -> p k h", p=P)).then_inc(l_w[b], 16)
                act.dma_start(w2s[b][:, :, :], e_w2[b].rearrange("(m p) d -> p m d", p=P)).then_inc(l_w[b], 16)
            act.dma_start(epsb[:, :], eps.rearrange("(a e) -> a e", a=1).broadcast_to((P, 1))).then_inc(l_small, 16)

            def normalise(t, ready, done):
                act.activation(xn[:, t, 0:D], x_sb[:, t, :], ACT.Identity,
                               bias=nbias[:, t:t + 1], scale=rstd[:, t:t + 1]).then_inc(done, 1)

            for q in range(NPIECE):
                act.wait_ge(rstd_ready, q + 1)
                for t in range(q * PIECE, (q + 1) * PIECE):
                    normalise(t, rstd_ready, xn_ready)

            act.wait_ge(table_ready, 1)
            act.wait_ge(consts, 5)
            with act.Fori(0, G // SLOTS) as i:
                for s in range(SLOTS):
                    g = i * SLOTS + s
                    s0 = table(act, tab_step, g, 1, MAXSTEP)
                    s1 = table(act, tab_step, g + 1, 1, MAXSTEP)
                    act.wait_ge(slot_free, g + 1)
                    act.activation(idx[s][:, :], srcT[:, bass.ds(g * CH, CH)], ACT.Copy).then_inc(idx_ready, 1)

                    def one_hot(step, first):
                        for c in range(CH):
                            cols = iota_n[:, 0:W] if first else iota_n[:, bass.ds(window(0, step, s0, NP - W), W)]
                            act.activation(near[s][:, c, :], cols, ACT.Abs,
                                           bias=below[:, bass.ds(g * CH + c, 1)]).then_inc(near_ready, 1)
                        act.wait_ge(near_ready, step * CH)
                        act.activation(onehot[s][:, :, :], near[s][:, :, :], ACT.Relu, scale=-1.0, bias=1.0)\
                           .then_inc(onehot_ready, 1)

                    def extra(step):
                        act.wait_ge(win_done, step)
                        one_hot(step, False)

                    one_hot(s0, True)
                    extra_steps(act, s0, s1, extra)

            act.wait_ge(bias_ready, 1)
            act.sem_inc(relu_done, GM)

            def relus(n):
                for m in range(GM):
                    act.wait_ge(mm1_done, n * GM + m + 1)
                    act.activation(hid[:, m, :], ps[m][:, 0:MC], ACT.Relu, bias=bcol[:, B_G1 + m:B_G1 + m + 1])\
                       .then_inc(relu_done, 1)

            with act.Fori(0, MG) as n:
                relus(n)

            act.wait_ge(bn_ready, 1)
            for q in range(NPIECE):
                for k in range(K):
                    cols = slice(q * PIECE * P, (q + 1) * PIECE * P)
                    act.activation(agg[:, k, cols], agg[:, k, cols], ACT.Identity,
                                   bias=bnsh[:, k:k + 1], scale=bnsc[:, k:k + 1]).then_inc(bn_applied, 1)
            for q in range(NPIECE):
                act.wait_ge(rstd2_ready, q + 1)
                if q == 0:
                    act.wait_ge(xn_T, T)
                for t in range(q * PIECE, (q + 1) * PIECE):
                    normalise(t, rstd2_ready, xn2_ready)
                    if t >= 2:
                        copy_xT(act, t - 2)
            for t in range(T - 2, T):
                copy_xT(act, t)
            act.wait_ge(diff_ready, 1)
            act.activation(ex[:, :], v2[:, :], ACT.Exp).then_inc(exp_ready, 1)

            act.wait_ge(route_ready, 1)
            act.sem_inc(gelu_done, EM)
            for e in range(NE):
                b = e % 2
                if 1 <= e < NE - 1:
                    nb = (e + 1) % 2
                    act.wait_ge(expert_done, e)
                    act.dma_start(w1s[nb][:, :, :], e_w1[e + 1].rearrange("(k p) h -> p k h", p=P)).then_inc(l_w[nb], 16)
                    act.dma_start(w2s[nb][:, :, :], e_w2[e + 1].rearrange("(m p) d -> p m d", p=P)).then_inc(l_w[nb], 16)
                j0 = table(act, tab_tile, e, 1, MAXTILE)
                j1 = table(act, tab_tile, e + 1, 1, MAXTILE)
                with act.Fori(j0, j1) as j:
                    for m in range(EM):
                        act.wait_ge(e_mm1, j * EM + m + 1)
                        act.activation(hT[:, m, :], ps[m % 4][:, 0:RT], ACT.Gelu,
                                       bias=bcol[:, e * EM + m:e * EM + m + 1]).then_inc(gelu_done, 1)

        @block.vector
        def _(dve):
            chain = [0]

            def link(ins):
                chain[0] += 1
                ins.then_inc(dve_seq, 1)
                dve.wait_ge(dve_seq, chain[0])

            dve.memset(x_sb[:, T - 1, :], 0.0).then_inc(x_pad_set, 1)
            dve.memset(agg[:, :, NP:NP + W], 0.0).then_inc(agg_set, 1)
            dve.wait_ge(l_edges, 64)
            dve.wait_ge(consts, 5)
            dve.tensor_copy(src_f[:, :], src_i[:, :]).then_inc(src_ready, 1)
            link(dve.tensor_copy(dst_f[:, :], dst_i[:, :]))
            dve.tensor_reduce(dminmax[:, 0:1], dst_f[:, :], AX.X, ALU.min).then_inc(dst_ready, 1)
            link(dve.scalar_tensor_tensor(out=dst_real[:, :], in0=dst_f[:, :], scalar=float(NP), in1=dst_f[:, :],
                                          op0=ALU.is_lt, op1=ALU.mult))
            dve.wait_ge(dst_ready, 1)
            link(dve.tensor_reduce(dminmax[:, 1:2], dst_real[:, :], AX.X, ALU.max))
            for k in range(2):
                dve.tensor_scalar(dspread[:, k, :], ones[0:G, :], dminmax[:, k:k + 1], None, ALU.mult).then_inc(dst_ready, 1)

            def row_stats(q, done):
                for t in range(q * PIECE, (q + 1) * PIECE):
                    ins = dve.bn_stats(stats[:, t, :], x_sb[:, t, :])
                link(ins)
                for t in range(q * PIECE, (q + 1) * PIECE):
                    dve.bn_aggr(mv[:, t, :], stats[:, t, :]).then_inc(done, 1)

            def set_agg(t):
                dve.wait_ge(xn_T, t + 1)
                dve.tensor_scalar(agg[:, :, t * P:(t + 1) * P],
                                  ps[4 + t % 4][:, 0:K * P].rearrange("p (k c) -> p k c", c=P),
                                  self_w[:, 0:1], None, ALU.mult).then_inc(agg_set, 1)

            dve.wait_ge(l_small, 16 * 8)
            self_w = epsb
            link(dve.tensor_scalar_add(epsb[:, :], epsb[:, :], 1.0))
            for q in range(NPIECE):
                dve.wait_ge(l_x[q], 32 if q == NPIECE - 1 else 16)
                row_stats(q, mv_ready)

            dve.wait_ge(lists_T, 3)
            dst_T = ps[0][:, 0:CH * G].rearrange("p (c g) -> p g c", g=G)
            src_T = ps[1][:, 0:CH * G].rearrange("p (c g) -> p g c", g=G)
            link(dve.tensor_copy(srcT[:, :].rearrange("p (g c) -> p g c", c=CH), src_T))
            link(dve.tensor_copy(wmin[:, :], ps[2][:, 0:G]))
            link(dve.tensor_copy(below[:, :].rearrange("p (g c) -> p g c", c=CH), dst_T))
            link(dve.tensor_tensor(below[:, :].rearrange("p (g c) -> p g c", c=CH),
                                   wmin[:, :].unsqueeze(2).broadcast_to((P, G, CH)),
                                   below[:, :].rearrange("p (g c) -> p g c", c=CH), ALU.subtract))
            link(dve.tensor_tensor(span[:, :], ps[2][:, 128:128 + G], wmin[:, :], ALU.subtract))
            link(dve.tensor_copy(tab_win[:, :], span[:, :]))
            link(dve.tensor_scalar(tab_win[:, :], tab_win[:, :], W.bit_length() - 1, None, ALU.arith_shift_right))
            link(dve.tensor_copy(span[:, :], tab_win[:, :]))
            link(dve.tensor_scalar_add(steps[:, :], span[:, :], 1.0))
            link(dve.tensor_tensor_scan(rem[:, :], ones[:, 0:G], steps[:, :], 1.0, ALU.mult, ALU.add))
            link(dve.memset(tab_step[:, 0:1], 1))
            link(dve.tensor_copy(tab_step[:, 1:G + 1], rem[:, :]))
            link(dve.tensor_copy(tab_win[:, :], wmin[:, :]))
            dve.wait_ge(bias_T, 1)
            dve.tensor_copy(bcol[:, :], ps[3][:, 0:NB]).then_inc(bias_ready, 1)
            dve.wait_ge(bias_ready, 1)
            dve.sem_inc(table_ready, 1)
            for t in range(T):
                set_agg(t)

            dve.wait_ge(agg_set, T + 1)
            dve.sem_inc(slot_free, SLOTS)
            dve.sem_inc(win_done, 1)
            with dve.Fori(0, G // SLOTS) as i:
                for s in range(SLOTS):
                    g = i * SLOTS + s
                    s0 = table(dve, tab_step, g, 1, MAXSTEP)
                    s1 = table(dve, tab_step, g + 1, 1, MAXSTEP)
                    w0 = table(dve, tab_win, g, 0, NP - 1)

                    def add(step):
                        cols = bass.ds(window(w0, step, s0, NP), W)
                        dve.wait_ge(win_mm, step)
                        dve.wait_ge(win_done, step)
                        dve.tensor_tensor(agg[:, :, cols], agg[:, :, cols],
                                          ps[s][:, 0:K * W].rearrange("p (k w) -> p k w", w=W), ALU.add)\
                           .then_inc(win_done, 1)

                    add(s0)
                    extra_steps(dve, s0, s1, add)
                    dve.wait_ge(win_done, s1)
                    dve.sem_inc(slot_free, 1)

            dve.sem_inc(h_done, K)

            def h_out(n, real):
                for k in range(K):
                    cols = bass.ds(n * MC, MC)
                    dve.wait_ge(mm2_done, n * K + k + 1)
                    dve.tensor_scalar(agg[:, k, cols], ps[4 + k][:, 0:MC], bcol[:, B_G2 + k:B_G2 + k + 1], None, ALU.add)\
                       .then_inc(h_done, 1)
                for k in range(K):
                    dve.wait_ge(h_done, n * K + K + k + 1)
                    dve.bn_stats(bnst[:, k, bass.ds(n, 1), :].rearrange("p a b -> p (a b)"),
                                 agg[:, k, bass.ds(n * MC, real)]).then_inc(bn_chunks, 1)

            with dve.Fori(0, MG - 1) as n:
                h_out(n, MC)
            h_out(MG - 1, MLAST)
            dve.wait_ge(bn_chunks, K * MG)
            for k in range(K):
                dve.bn_aggr(bnmv[:, k, :], bnst[:, k, :, :].rearrange("p a b -> p (a b)")).then_inc(bn_var, 1)
            dve.wait_ge(bn_rstd, 1)
            link(dve.tensor_tensor(bnsc[:, :], bnsc[:, :], bcol[:, B_GA:B_GA + K], ALU.mult))
            link(dve.tensor_tensor(bnsh[:, :], bnmv[:, :, 0], bnsc[:, :], ALU.mult))
            dve.tensor_tensor(bnsh[:, :], bcol[:, B_BE:B_BE + K], bnsh[:, :], ALU.subtract).then_inc(bn_ready, 1)

            for q in range(NPIECE):
                for t in range(q * PIECE, (q + 1) * PIECE):
                    dve.wait_ge(h_T, t + 1)
                    dve.tensor_tensor(x_sb[:, t, :], x_sb[:, t, :], ps[t % 4][:, 0:D], ALU.add).then_inc(res_done, 1)
                dve.wait_ge(res_done, (q + 1) * PIECE)
                row_stats(q, mv2_ready)

            dve.wait_ge(gate_done, T)
            all_e = (P, T, NE)
            rk = rank_e[:, :].unsqueeze(1).broadcast_to(all_e)
            vd = valid[:, :].unsqueeze(2).broadcast_to(all_e)
            link(dve.tensor_tensor(lg[:, :, :], ps[7][:, 0:T * NE].rearrange("p (t e) -> p t e", e=NE),
                                   bgb[:, :].unsqueeze(1).broadcast_to(all_e), ALU.add))

            def choose(logits, v, r, m):
                link(dve.tensor_reduce(v[:, :], logits[:, :, :], AX.X, ALU.max))
                link(dve.tensor_tensor(eqs[:, :, :], logits[:, :, :], v[:, :].unsqueeze(2).broadcast_to(all_e), ALU.is_equal))
                link(dve.tensor_tensor(eqs[:, :, :], eqs[:, :, :], rk, ALU.mult))
                link(dve.tensor_reduce(r[:, :], eqs[:, :, :], AX.X, ALU.max))
                link(dve.tensor_tensor(m[:, :, :], rk, r[:, :].unsqueeze(2).broadcast_to(all_e), ALU.is_equal))

            choose(lg, v1, r1, m1)
            link(dve.scalar_tensor_tensor(out=lg2[:, :, :], in0=m1[:, :, :], scalar=-3.0e38, in1=lg[:, :, :],
                                          op0=ALU.mult, op1=ALU.add))
            choose(lg2, v2, r2, m2)
            dve.tensor_tensor(v2[:, :], v2[:, :], v1[:, :], ALU.subtract).then_inc(diff_ready, 1)
            link(dve.tensor_tensor(m1[:, :, :], m1[:, :, :], vd, ALU.mult))
            link(dve.tensor_tensor(m2[:, :, :], m2[:, :, :], vd, ALU.mult))
            dve.tensor_tensor(msum[:, :, :], m1[:, :, :], m2[:, :, :], ALU.add).then_inc(mask_ready, 1)
            dve.wait_ge(exp_ready, 1)
            link(dve.tensor_scalar_add(w1v[:, :], ex[:, :], 1.0))
            link(dve.reciprocal(w1v[:, :], w1v[:, :]))
            link(dve.tensor_tensor(w2v[:, :], ex[:, :], w1v[:, :], ALU.mult))
            link(dve.tensor_copy(xn[:, :, META + 0], w1v[:, :]))
            link(dve.tensor_copy(xn[:, :, META + 1], w2v[:, :]))
            link(dve.tensor_scalar(xn[:, :, META + 2], r1[:, :], -1.0, float(NE), ALU.mult, ALU.add))
            link(dve.tensor_copy(xn[:, :, META + 3], tok[:, :]))
            dve.wait_ge(rank_mm, 2)
            link(dve.tensor_copy(tot[:, :, :], ps[6][:, 256:256 + T * NE].rearrange("p (t e) -> p t e", e=NE)))
            for e in range(NE):
                last = dve.tensor_tensor_scan(incl[:, :, e], ones[:, 0:T], tot[:, :, e], 0.0, ALU.mult, ALU.add)
            link(last)
            link(dve.tensor_tensor(posn[:, :, :], incl[:, :, :], tot[:, :, :], ALU.subtract))
            link(dve.tensor_tensor(posn[:, :, :], posn[:, :, :],
                                   ps[6][:, 0:T * NE].rearrange("p (t e) -> p t e", e=NE), ALU.add))
            link(dve.tensor_tensor(posn[:, :, :], posn[:, :, :], eoff[:, :].unsqueeze(1).broadcast_to(all_e), ALU.add))
            link(dve.tensor_scalar(novalid[:, :], valid[:, :], -BIG, BIG, ALU.mult, ALU.add))
            for k, m in ((0, m1), (1, m2)):
                link(dve.tensor_tensor(eqs[:, :, :], m[:, :, :], posn[:, :, :], ALU.mult))
                link(dve.tensor_reduce(posf[:, k, :], eqs[:, :, :], AX.X, ALU.add))
                link(dve.tensor_tensor(posf[:, k, :], posf[:, k, :], novalid[:, :], ALU.add))
            link(dve.tensor_copy(posi[:, :, :], posf[:, :, :]))
            link(dve.tensor_copy(cnt[:, :], incl[:, T - 1, :]))
            link(dve.tensor_tensor(padf[:, :], cnt[:, :], eoff[:, :], ALU.add))
            link(dve.tensor_copy(tab_pad[:, :], padf[:, :]))
            link(dve.tensor_scalar(cnt[:, :], cnt[:, :], 1.0, float(RT - 1), ALU.max, ALU.add))
            link(dve.tensor_copy(tab_tile[:, 0:NE], cnt[:, :]))
            link(dve.tensor_scalar(tab_tile[:, 0:NE], tab_tile[:, 0:NE], RT.bit_length() - 1, None, ALU.arith_shift_right))
            link(dve.tensor_copy(cnt[:, :], tab_tile[:, 0:NE]))
            link(dve.tensor_tensor_scan(ntl[:, :], ones[:, 0:NE], cnt[:, :], 1.0, ALU.mult, ALU.add))
            link(dve.memset(tab_tile[:, 0:1], 1))
            link(dve.tensor_copy(tab_tile[:, 1:NE + 1], ntl[:, :]))
            dve.sem_inc(route_ready, 1)

            dve.sem_inc(meta_ready, 1)

            def take_tile(j, jm):
                dve.wait_ge(xs_T, jm + 1)
                dve.tensor_copy(xsT[:, :, :].rearrange("p k c -> p (k c)"), ps[4][:, :]).then_inc(xsT_ready, 1)
                dve.wait_ge(ybuf_free, j)
                dve.tensor_copy(meta[:, bass.ds(jm % 2, 1), :].rearrange("p o (a c) -> p (o a) c", c=4),
                                xs[:, :, META:META + 4]).then_inc(meta_ready, 1)

            dve.wait_ge(l_gw, 48)
            dve.sem_inc(y_seq, RH)
            dve.sem_inc(wsel_ready, WOPS)
            take_tile(1, 1)
            for e in range(NE):
                j0 = table(dve, tab_tile, e, 1, MAXTILE)
                j1 = table(dve, tab_tile, e + 1, 1, MAXTILE)
                with dve.Fori(j0, j1) as j:
                    take_tile(j, j + 1)
                    mt = meta[:, bass.ds(j % 2, 1), :].rearrange("p o (a c) -> p (o a) c", c=4)
                    base = j * WOPS
                    dve.wait_ge(meta_ready, j + 1)
                    dve.tensor_scalar(is1[:, :], mt[:, :, 2], float(e), None, ALU.is_equal).then_inc(wsel_ready, 1)
                    dve.wait_ge(wsel_ready, base + 1)
                    dve.tensor_scalar(not1[:, :], is1[:, :], -1.0, 1.0, ALU.mult, ALU.add).then_inc(wsel_ready, 1)
                    dve.tensor_tensor(wa[:, :], is1[:, :], mt[:, :, 0], ALU.mult).then_inc(wsel_ready, 1)
                    dve.wait_ge(wsel_ready, base + 3)
                    dve.tensor_tensor(wsel[:, :], not1[:, :], mt[:, :, 1], ALU.mult).then_inc(wsel_ready, 1)
                    dve.scalar_tensor_tensor(out=dest[:, :], in0=not1[:, :], scalar=float(NP), in1=mt[:, :, 3],
                                             op0=ALU.mult, op1=ALU.add).then_inc(wsel_ready, 1)
                    dve.wait_ge(wsel_ready, base + 5)
                    dve.tensor_tensor(wsel[:, :], wsel[:, :], wa[:, :], ALU.add).then_inc(wsel_ready, 1)
                    dve.tensor_copy(desti[:, :], dest[:, :]).then_inc(wsel_ready, 1)
                    dve.wait_ge(e_mm2, j + 1)
                    for a in range(RH):
                        dve.tensor_tensor(ytmp[:, a, :], ps[5 + a][:, 0:D], b2b[:, e, :], ALU.add).then_inc(y_seq, 1)
                    dve.wait_ge(y_seq, (j + 1) * RH)
                    dve.wait_ge(wsel_ready, (j + 1) * WOPS)
                    for a in range(RH):
                        ins = dve.tensor_scalar(ysb[:, a, :], ytmp[:, a, :], wsel[:, a:a + 1], None, ALU.mult)
                    ins.then_inc(y_ready, 1)

            for q in range(NPIECE):
                t0, t1 = q * PIECE, (q + 1) * PIECE
                dve.wait_ge(y_in[q], 64 if q == NPIECE - 1 else 32)
                for y in y_pair(t0, t1):
                    link(dve.tensor_tensor(x_sb[:, t0:t1, :], x_sb[:, t0:t1, :], y, ALU.add))
                dve.sem_inc(out_ready, 1)

        @block.tensor
        def _(pe):
            pe.wait_ge(consts, 5)
            pe.wait_ge(src_ready, 1)
            pe.wait_ge(dst_ready, 3)
            for b, lst in ((0, dst_f), (1, src_f)):
                for c in range(CH):
                    ins = pe.transpose(ps[b][:, c * G:(c + 1) * G], lst[:, c * P:(c + 1) * P], ident[0:G, 0:G])
                ins.then_inc(lists_T, 1)
            for k in range(2):
                ins = pe.matmul(ps[2][:, k * P:k * P + G], dspread[:, k, :], ident[0:G, 0:G], start=True, stop=True)
            ins.then_inc(lists_T, 1)
            pe.wait_ge(l_small, 16 * 8)
            pe.transpose(ps[3][:, 0:NB], brows[:, :], ident[0:NB, 0:NB]).then_inc(bias_T, 1)

            def transpose_rows(t, bank, done):
                for k in range(K):
                    ins = pe.transpose(ps[bank][:, k * P:(k + 1) * P], xn[:, t, k * P:(k + 1) * P], ident[:, :])
                ins.then_inc(done, 1)

            for t in range(T):
                pe.wait_ge(xn_ready, t + 1)
                if t >= 4:
                    pe.wait_ge(agg_set, t - 2)
                transpose_rows(t, 4 + t % 4, xn_T)

            pe.wait_ge(table_ready, 1)
            with pe.Fori(0, G // SLOTS) as i:
                for s in range(SLOTS):
                    g = i * SLOTS + s
                    s0 = table(pe, tab_step, g, 1, MAXSTEP)
                    s1 = table(pe, tab_step, g + 1, 1, MAXSTEP)

                    def product(step):
                        pe.wait_ge(onehot_ready, step)
                        for k in range(K):
                            for c in range(CH):
                                ins = pe.matmul(ps[s][:, k * W:(k + 1) * W], rows[s][:, c, k * P:(k + 1) * P],
                                                onehot[s][:, c, :], start=(c == 0), stop=(c == CH - 1))
                        ins.then_inc(win_mm, 1)

                    pe.wait_ge(rows_in[s], (i + 1) * (16 * CH))
                    product(s0)
                    extra_steps(pe, s0, s1, product)

            pe.wait_ge(slot_free, SLOTS + G)
            pe.wait_ge(l_gw, 48)
            with pe.Fori(0, MG) as n:
                for m in range(GM):
                    pe.wait_ge(relu_done, n * GM + m + 1)
                    for k in range(K):
                        ins = pe.matmul(ps[m][:, 0:MC], gw1[:, k, m * P:(m + 1) * P], agg[:, k, bass.ds(n * MC, MC)],
                                        start=(k == 0), stop=(k == K - 1))
                    ins.then_inc(mm1_done, 1)
                for k in range(K):
                    pe.wait_ge(h_done, n * K + k + 1)
                    for m in range(GM):
                        pe.wait_ge(relu_done, n * GM + GM + m + 1)
                        ins = pe.matmul(ps[4 + k][:, 0:MC], gw2[:, m, k * P:(k + 1) * P], hid[:, m, :],
                                        start=(m == 0), stop=(m == GM - 1))
                    ins.then_inc(mm2_done, 1)

            def gate(t):
                pe.wait_ge(xT_ready, t + 1)
                for k in range(K):
                    ins = pe.matmul(ps[7][:, t * NE:(t + 1) * NE], xT[t % 2][:, k, :], wgs[:, k, :],
                                    start=(k == 0), stop=(k == K - 1))
                ins.then_inc(gate_done, 1)

            for q in range(NPIECE):
                pe.wait_ge(bn_applied, (q + 1) * K)
                for t in range(q * PIECE, (q + 1) * PIECE):
                    if t >= 4:
                        pe.wait_ge(res_done, t - 3)
                    for k in range(K):
                        ins = pe.transpose(ps[t % 4][:, k * P:(k + 1) * P], agg[:, k, t * P:(t + 1) * P], ident[:, :])
                    ins.then_inc(h_T, 1)
            pe.wait_ge(h_done, K + K * MG)
            for t in range(T):
                pe.wait_ge(xn2_ready, t + 1)
                if t >= 2:
                    pe.wait_ge(xT_ready, t - 1)
                transpose_rows(t, 4 + t % 2, xn2_T)
                if t >= 1:
                    gate(t - 1)
            gate(T - 1)

            pe.wait_ge(mask_ready, 1)
            pe.matmul(ps[6][:, 0:T * NE], upper[:, :], msum[:, :, :].rearrange("p t e -> p (t e)"),
                      start=True, stop=True).then_inc(rank_mm, 1)
            pe.matmul(ps[6][:, 256:256 + T * NE], ones[:, :], msum[:, :, :].rearrange("p t e -> p (t e)"),
                      start=True, stop=True).then_inc(rank_mm, 1)

            def transpose_tile(jm):
                pe.wait_ge(xs_in, jm * 16)
                for a in range(RH):
                    for k in range(K):
                        ins = pe.transpose(ps[4][:, k * RT + a * P:k * RT + (a + 1) * P],
                                           xs[:, a, k * P:(k + 1) * P], ident[:, :])
                ins.then_inc(xs_T, 1)

            pe.wait_ge(route_ready, 1)
            pe.sem_inc(xs_T, 1)
            pe.sem_inc(e_mm1, EM)
            pe.sem_inc(e_mm2, 1)
            transpose_tile(1)
            for e in range(NE):
                b = e % 2
                j0 = table(pe, tab_tile, e, 1, MAXTILE)
                j1 = table(pe, tab_tile, e + 1, 1, MAXTILE)
                pe.wait_ge(l_w[b], 32 * (e // 2 + 1))
                with pe.Fori(j0, j1) as j:
                    pe.wait_ge(xsT_ready, j)
                    for m in range(EM):
                        if m >= 4:
                            pe.wait_ge(gelu_done, j * EM + m - 3)
                        for k in range(K):
                            ins = pe.matmul(ps[m % 4][:, 0:RT], w1s[b][:, k, m * P:(m + 1) * P], xsT[:, k, :],
                                            start=(k == 0), stop=(k == K - 1))
                        ins.then_inc(e_mm1, 1)
                    transpose_tile(j + 1)
                    pe.wait_ge(y_seq, j * RH)
                    for m in range(EM):
                        pe.wait_ge(gelu_done, j * EM + m + 1)
                        for a in range(RH):
                            ins = pe.matmul(ps[5 + a][:, 0:D], hT[:, m, a * P:(a + 1) * P], w2s[b][:, m, :],
                                            start=(m == 0), stop=(m == EM - 1))
                    ins.then_inc(e_mm2, 1)
                pe.wait_ge(e_mm2, j1)
                pe.sem_inc(expert_done, 1)


_INS = ['x', 'src', 'dst', 'L0_gnn_eps', 'L0_gnn_W1', 'L0_gnn_b1', 'L0_gnn_W2', 'L0_gnn_b2', 'L0_gnn_gamma',
        'L0_gnn_beta', 'L0_ffn_Wg', 'L0_ffn_bg', 'L0_ffn_W1', 'L0_ffn_b1', 'L0_ffn_W2', 'L0_ffn_b2']


def kernel(**inputs):
    import numpy as np
    import concourse.bacc as bacc
    from concourse import mybir
    from concourse.bass_utils import run_bass_kernel_spmd

    nc = bacc.Bacc("TRN2", target_bir_lowering=False, num_devices=1)
    arrays, args = {}, []
    for name in _INS:
        a = np.ascontiguousarray(inputs[name])
        arrays[f"in_{name}"] = a
        args.append(nc.dram_tensor(f"in_{name}", a.shape, mybir.dt.from_np(a.dtype), kind="ExternalInput").ap())
    x = inputs['x']
    args.append(nc.dram_tensor("out_x", x.shape, mybir.dt.from_np(np.dtype('float32')), kind="ExternalOutput").ap())
    gnn_moe_block(nc, *args)
    r = run_bass_kernel_spmd(nc, [arrays], core_ids=[0])
    return r.results[0]["out_x"]
```
